# Optimizing a Trainium2 kernel written in Bass

```python
import numpy as np
import jax
import jax.numpy as jnp

def _softmax(x, axis=-1):
    return jax.nn.softmax(x, axis=axis)

def _gelu(x):
    return jax.nn.gelu(x, approximate=True)

def _silu(x):
    return jax.nn.silu(x)

def _sigmoid(x):
    return jax.nn.sigmoid(x)

def _layernorm(x, axis=-1, eps=1e-05):
    m = jnp.mean(x, axis=axis, keepdims=True)
    v = jnp.var(x, axis=axis, keepdims=True)
    return (x - m) / jnp.sqrt(v + eps)

def _scatter_add(tgt, idx, src, axis=0):
    return tgt.at[idx].add(src)

def _segment_sum(src, seg, n):
    return jax.ops.segment_sum(src, seg, n)
kernel_name = 'mk_gnn_resnorm_d1_gnn_r8_fd16ab'

def setup_inputs(seed: int=0):
    np.random.seed(seed)
    _w = jnp.asarray

    def _rec_inputs():
        import jax
        import jax.numpy as jnp
        _gk = jax.random.key(seed)
        x = -0.0001006 + 1 * jax.random.normal(jax.random.fold_in(_gk, 1), (6250, 96), jnp.float32)
        _s = jax.random.randint(jax.random.fold_in(_gk, 2), (100000,), 0, 6250, jnp.int32)
        _d = jax.random.randint(jax.random.fold_in(_gk, 3), (100000,), 0, 6250, jnp.int32)
        _loop = jnp.arange(6250, dtype=jnp.int32)
        src = jnp.concatenate([_s, _d, _loop])
        dst = jnp.concatenate([_d, _s, _loop])
        _o = jnp.argsort(dst, stable=True)
        src = src[_o]
        dst = dst[_o]
        edge_attr_96 = 5.93493e-05 + 1.00006 * jax.random.normal(jax.random.fold_in(_gk, 11), (206250, 96), jnp.float32)
        return (x, src, dst, edge_attr_96)
    x, src, dst, edge_attr_96 = _rec_inputs()

    def _L0_gnn_setup():
        import jax, jax.numpy as jnp
        import numpy as np
        N_NODES = 6250
        N_EDGES = 100000
        IN_DIM = 96
        NUM_HEADS = 8
        HEAD_DIM = IN_DIM // NUM_HEADS
        key = jax.random.key(seed)
        ks = jax.random.split(key, 11)
        s = 1.0 / np.sqrt(IN_DIM)
        return {'x': jax.random.normal(ks[0], (N_NODES, IN_DIM), dtype=jnp.float32), 'edge_index': jax.random.randint(ks[1], (2, N_EDGES), 0, N_NODES, dtype=jnp.int64), 'edge_attr': jax.random.normal(ks[2], (N_EDGES, IN_DIM), dtype=jnp.float32), 'Wq': jax.random.normal(ks[3], (IN_DIM, IN_DIM), dtype=jnp.float32) * s, 'bq': jax.random.normal(ks[4], (IN_DIM,), dtype=jnp.float32) * s, 'Wk': jax.random.normal(ks[5], (IN_DIM, IN_DIM), dtype=jnp.float32) * s, 'bk': jax.random.normal(ks[6], (IN_DIM,), dtype=jnp.float32) * s, 'We': jax.random.normal(ks[7], (IN_DIM, IN_DIM), dtype=jnp.float32) * s, 'be': jax.random.normal(ks[8], (IN_DIM,), dtype=jnp.float32) * s, 'Wv': jax.random.normal(ks[9], (IN_DIM, IN_DIM), dtype=jnp.float32) * s, 'bv': jax.random.normal(ks[10], (IN_DIM,), dtype=jnp.float32) * s}
    _L0_gnn_all = _L0_gnn_setup()
    _L0_gnn_in = {k: v for k, v in _L0_gnn_all.items() if k in ('Wq', 'bq', 'Wk', 'bk', 'We', 'be', 'Wv', 'bv')}
    del _L0_gnn_all
    return {'x': x, 'src': src, 'dst': dst, 'edge_attr_96': edge_attr_96, 'L0_gnn_Wq': _L0_gnn_in['Wq'], 'L0_gnn_bq': _L0_gnn_in['bq'], 'L0_gnn_Wk': _L0_gnn_in['Wk'], 'L0_gnn_bk': _L0_gnn_in['bk'], 'L0_gnn_We': _L0_gnn_in['We'], 'L0_gnn_be': _L0_gnn_in['be'], 'L0_gnn_Wv': _L0_gnn_in['Wv'], 'L0_gnn_bv': _L0_gnn_in['bv']}

def reference(x, src, dst, edge_attr_96, L0_gnn_Wq, L0_gnn_bq, L0_gnn_Wk, L0_gnn_bk, L0_gnn_We, L0_gnn_be, L0_gnn_Wv, L0_gnn_bv):
    import jax
    import jax.numpy as jnp

    def _L0_gnn_ref(x, edge_index, edge_attr, Wq, bq, Wk, bk, We, be, Wv, bv):
        import jax, jax.numpy as jnp
        import numpy as np
        N_NODES = 6250
        N_EDGES = 100000
        IN_DIM = 96
        NUM_HEADS = 8
        HEAD_DIM = IN_DIM // NUM_HEADS
        N = x.shape[0]
        H, D = (NUM_HEADS, HEAD_DIM)
        Q_h = (x @ Wq + bq).reshape(N, H, D)
        K_h = (x @ Wk + bk).reshape(N, H, D)
        V_h = (x @ Wv + bv).reshape(N, H, D)
        E = (edge_attr @ We + be).reshape(-1, H, D)
        src_idx = edge_index[0]
        dst_idx = edge_index[1]
        src = K_h[src_idx]
        dest = Q_h[dst_idx]
        score = src * dest / jnp.sqrt(jnp.asarray(D, x.dtype))
        score = score * E
        score = jnp.exp(jnp.clip(score.sum(-1, keepdims=True), -5.0, 5.0))
        msg = V_h[src_idx] * score
        wV = jax.ops.segment_sum(msg, dst_idx, num_segments=N)
        Z = jax.ops.segment_sum(score, dst_idx, num_segments=N)
        h_out = wV / (Z + 1e-06)
        return h_out.reshape(N, H * D)
    edge_index = jnp.stack([src, dst])
    x = _layernorm(x + _L0_gnn_ref(x, edge_index, edge_attr_96, L0_gnn_Wq, L0_gnn_bq, L0_gnn_Wk, L0_gnn_bk, L0_gnn_We, L0_gnn_be, L0_gnn_Wv, L0_gnn_bv), axis=-1)
    return x

_drawn_inputs = setup_inputs


def setup_inputs(seed=0):
    import zlib

    import numpy as np

    out = dict(_drawn_inputs(seed))
    spreads = {}
    factors = {}
    for name, (base, spread) in spreads.items():
        noise = np.random.default_rng([zlib.crc32(name.encode()), seed]).standard_normal(out[name].shape)
        drawn = base * np.exp(spread * noise) if base else spread * noise
        out[name] = jnp.asarray(drawn.astype(out[name].dtype))
    for name, factor in factors.items():
        out[name] = (out[name] * factor).astype(out[name].dtype)
    return out
```

```python
import concourse.bass as bass
from concourse import mybir
from contextlib import ExitStack

NODES = 6250
EDGES = 206250
DIM = 96
HEADS = 8
HEAD_DIM = DIM // HEADS
MSG = DIM + HEADS

P = 128
TILE = 128
TILES = -(-EDGES // TILE)
GROUP_TILES = 4
GROUP = GROUP_TILES * TILE
GROUPS = TILES // GROUP_TILES
SLOTS = 4
WINDOW = 32
LOOP_ITERATIONS = GROUPS // SLOTS
SLOT_GROUPS = [len(range(s, GROUPS, SLOTS)) for s in range(SLOTS)]

NODE_TILES = 50
NODE_PARTITIONS = NODES // NODE_TILES
NODES_PAD = P * NODE_TILES
CHUNK = 5
CHUNKS = NODE_TILES // CHUNK
LAST_WINDOW = -(-NODES // WINDOW) * WINDOW
MAX_PASSES = LAST_WINDOW // WINDOW
CLIP = 5.0 * HEAD_DIM ** 0.5
SCALE = HEAD_DIM ** -0.5
assert TILES % GROUP_TILES == 0 and NODES % NODE_TILES == 0 and LAST_WINDOW + WINDOW <= NODES_PAD


def gnn_resnorm(nc, x_tiles, x_rows, edge_tiles, src, dst, first_dst, weights, out):
    fp32 = mybir.dt.float32
    int32 = mybir.dt.int32
    ALU = mybir.AluOpType
    ACT = mybir.ActivationFunctionType
    AX = mybir.AxisListType

    kv_table = nc.dram_tensor("kv_table", [NODES_PAD, 2 * DIM], fp32).ap()
    q_table = nc.dram_tensor("q_table", [NODES_PAD, DIM], fp32).ap()
    kv_table_tiles = kv_table.rearrange("(p t) d -> p t d", t=NODE_TILES)
    q_table_tiles = q_table.rearrange("(p t) d -> p t d", t=NODE_TILES)

    ctx = ExitStack()
    with ctx:
        def sb(name, shape, dt=fp32):
            return ctx.enter_context(nc.sbuf_tensor(name, shape, dt))

        def bank(name):
            return ctx.enter_context(nc.psum_tensor(name, [P, 512], fp32))

        def sem(name):
            return ctx.enter_context(nc.semaphore(name))

        w_all = sb("w_all", [DIM + 1, 4 * DIM])
        w_kvq = w_all[:, 0:3 * DIM]
        w_edge = w_all[:, 3 * DIM:4 * DIM]
        identity = sb("identity", [P, P])
        window_ids = sb("window_ids", [P, WINDOW])
        eps = sb("eps", [P, 1])
        src_sb = sb("src_sb", [P, TILES], int32)
        dst_sb = sb("dst_sb", [P, TILES], int32)
        first_sb = sb("first_sb", [P, GROUPS], int32)
        dst_f = sb("dst_f", [P, TILES])
        base_f = sb("base_f", [P, GROUPS])
        rel = sb("rel", [P, TILES])
        start_f = sb("start_f", [1, GROUPS])
        start_i = sb("start_i", [1, GROUPS], int32)
        low = sb("low", [P, 2])
        sorted_flag = sb("sorted_flag", [P, 1])
        high = sb("high", [P, 2])
        high_i = sb("high_i", [P, 1], int32)

        x_buf = [sb(f"x_buf{h}", [DIM + 1, CHUNK * P]) for h in range(2)]
        kv_stage = sb("kv_stage", [P, 2, CHUNK, 2 * DIM])
        q_stage = sb("q_stage", [P, 2, CHUNK, DIM])

        idx = [sb(f"idx{s}", [P, GROUP_TILES], int32) for s in range(SLOTS)]
        kv = [sb(f"kv{s}", [P, GROUP_TILES, 2 * DIM]) for s in range(SLOTS)]
        edge = [sb(f"edge{s}", [DIM + 1, GROUP]) for s in range(SLOTS)]
        q_diag = [sb(f"q_diag{s}", [P, GROUP_TILES * DIM]) for s in range(SLOTS)]
        hot = [sb(f"hot{s}", [P, GROUP_TILES, WINDOW]) for s in range(SLOTS)]
        hot_t = [sb(f"hot_t{b}", [P, TILE]) for b in range(2)]
        prod = sb("prod", [P, GROUP_TILES, DIM])
        score = sb("score", [P, GROUP_TILES * HEADS])
        clipped = [sb(f"clipped{b}", [P, GROUP_TILES, HEADS]) for b in range(2)]
        msg = [sb(f"msg{b}", [P, GROUP_TILES, MSG]) for b in range(2)]
        acc = sb("acc", [MSG, NODES_PAD])

        x_res = sb("x_res", [NODE_PARTITIONS, NODE_TILES, DIM])
        acc_tile = [sb(f"acc_tile{h}", [MSG, CHUNK, NODE_PARTITIONS]) for h in range(2)]
        z = [sb(f"z{h}", [NODE_PARTITIONS, CHUNK, HEADS]) for h in range(2)]
        rz = [sb(f"rz{h}", [NODE_PARTITIONS, CHUNK, HEADS]) for h in range(2)]
        attn = [sb(f"attn{h}", [NODE_PARTITIONS, CHUNK, DIM]) for h in range(2)]
        y = [sb(f"y{h}", [NODE_PARTITIONS, CHUNK, DIM]) for h in range(2)]
        stats = [sb(f"stats{h}", [NODE_PARTITIONS, CHUNK, 6]) for h in range(2)]
        mean_var = [sb(f"mean_var{h}", [NODE_PARTITIONS, CHUNK, 2]) for h in range(2)]
        std = [sb(f"std{h}", [NODE_PARTITIONS, CHUNK]) for h in range(2)]
        rstd = [sb(f"rstd{h}", [NODE_PARTITIONS, CHUNK]) for h in range(2)]
        shift = [sb(f"shift{h}", [NODE_PARTITIONS, CHUNK]) for h in range(2)]
        normed = [sb(f"normed{h}", [NODE_PARTITIONS, CHUNK, DIM]) for h in range(2)]

        banks = ctx.enter_context(nc.psum_tensor("banks", [P, 8, 512], fp32))
        hot_ps = [banks[:, b, 0:TILE] for b in range(2)]
        e_ps = [banks[:, 2 + b, 0:GROUP_TILES * DIM] for b in range(2)]
        q_ps = [banks[:, 4 + b, 0:GROUP_TILES * DIM] for b in range(2)]
        sum_ps = [banks[0:MSG, 6 + b, 0:WINDOW] for b in range(2)]
        table_ps = [banks[:, b, 0:3 * DIM] for b in range(CHUNK)]
        node_ps = [banks[0:NODE_PARTITIONS, 4 * h:4 * h + 4, :].rearrange("p a b -> p (a b)")[:, 0:CHUNK * P]
                   .rearrange("p (t d) -> p t d", d=P) for h in range(2)]

        weights_ready = sem("weights_ready")
        edges_ready = sem("edges_ready")
        first_ready = sem("first_ready")
        src_ready = sem("src_ready")
        residual_ready = sem("residual_ready")
        constants_ready = sem("constants_ready")
        x_ready = [sem(f"x_ready{h}") for h in range(2)]
        table_tile_ready = sem("table_tile_ready")
        table_tile_staged = sem("table_tile_staged")
        table_written = [sem(f"table_written{h}") for h in range(2)]
        ids_made = sem("ids_made")
        window_step = sem("window_step")
        low_ready = sem("low_ready")
        low_all_ready = sem("low_all_ready")
        high_ready = sem("high_ready")
        high_all_ready = sem("high_all_ready")
        passes_ready = sem("passes_ready")
        windows_ready = sem("windows_ready")

        idx_ready = sem("idx_ready")
        kv_ready = [sem(f"kv_ready{s}") for s in range(SLOTS)]
        edge_ready = [sem(f"edge_ready{s}") for s in range(SLOTS)]
        q_ready = [sem(f"q_ready{s}") for s in range(SLOTS)]
        hot_ready = sem("hot_ready")
        hot_ps_ready = sem("hot_ps_ready")
        hot_t_ready = sem("hot_t_ready")
        e_ps_ready = sem("e_ps_ready")
        q_ps_ready = sem("q_ps_ready")
        kq_done = sem("kq_done")
        kqe_done = sem("kqe_done")
        score_done = sem("score_done")
        clipped_ready = sem("clipped_ready")
        exp_ready = sem("exp_ready")
        msg_ready = sem("msg_ready")
        sum_ps_ready = sem("sum_ps_ready")
        acc_done = sem("acc_done")

        gathers_begun = sem("gathers_begun")
        acc_tiles_begun = sem("acc_tiles_begun")
        aggregates_begun = sem("aggregates_begun")
        acc_tile_ready = sem("acc_tile_ready")
        node_ps_ready = sem("node_ps_ready")
        node_step = sem("node_step")
        attn_ready = sem("attn_ready")
        var_ready = sem("var_ready")
        std_ready = sem("std_ready")
        shift_ready = sem("shift_ready")
        normed_ready = sem("normed_ready")
        y_ready = sem("y_ready")
        out_written = [sem(f"out_written{h}") for h in range(2)]

        def exists(i, u, k=0):
            return not isinstance(i, int) or 0 <= SLOTS * i + u + k < GROUPS

        def done(p, i, u, k=0):
            return p * GROUPS + i * SLOTS + (u + k + 1)

        def slot(u, k=0):
            return (u + k) % SLOTS

        def slot_uses(p, i, u, k=0):
            return p * SLOT_GROUPS[slot(u, k)] + i + ((u + k) // SLOTS + 1)

        def all_groups(eng, step, first, last):
            for g in range(first, SLOTS):
                step(g // SLOTS, g % SLOTS)
            with eng.Fori(1, LOOP_ITERATIONS) as i:
                for u in range(SLOTS):
                    step(i, u)
            for g in range(SLOTS * LOOP_ITERATIONS, last + 1):
                step(g // SLOTS, g % SLOTS)

        def number_of_passes(eng):
            eng.wait_ge(passes_ready, 1)
            greatest = eng.value_load(high_i[0:1, 0:1], min_val=0, max_val=LAST_WINDOW - 1)
            return eng.snap(greatest // WINDOW + 1)

        block = ctx.enter_context(nc.Block())

        @block.sync
        def _(sp):
            sp.dma_start(w_all[:, :], weights).then_inc(weights_ready, 16)
            for h in range(2):
                sp.dma_start(x_buf[h][0:DIM, :], x_tiles[h]).then_inc(x_ready[h], 16)
            sp.dma_start(dst_sb[:, :], dst).then_inc(edges_ready, 16)
            sp.dma_start(first_sb[:, :], first_dst.to_broadcast([P, GROUPS])).then_inc(first_ready, 16)
            sp.dma_start(src_sb[:, :], src).then_inc(src_ready, 16)

            def table_chunk(i, h):
                sp.wait_ge(table_tile_staged, CHUNK * (2 * i + h + 1))
                t = CHUNK * (2 * i + h)
                sp.dma_start(kv_table_tiles[:, bass.ds(t, CHUNK), :],
                             kv_stage[:, h, :, :]).then_inc(table_written[h], 16)
                sp.dma_start(q_table_tiles[:, bass.ds(t, CHUNK), :],
                             q_stage[:, h, :, :]).then_inc(table_written[h], 16)

            def load_x(i, h):
                sp.wait_ge(table_tile_ready, CHUNK * (2 * i + h + 1))
                sp.dma_start(x_buf[h][0:DIM, :],
                             x_tiles[bass.ds(2 * i + h + 2, 1)].rearrange("a d n -> (a d) n")
                             ).then_inc(x_ready[h], 16)

            with sp.Fori(0, CHUNKS // 2 - 1) as i:
                for h in range(2):
                    load_x(i, h)
                    table_chunk(i, h)
            for h in range(2):
                table_chunk(CHUNKS // 2 - 1, h)
            sp.dma_start(x_res[0:112], x_rows[0:112]).then_inc(residual_ready, 16)
            sp.dma_start(x_res[112:NODE_PARTITIONS], x_rows[112:NODE_PARTITIONS]).then_inc(residual_ready, 16)

            passes = number_of_passes(sp)
            for h in range(2):
                sp.wait_ge(table_written[h], 32 * (CHUNKS // 2))
            sp.wait_ge(constants_ready, 1)
            with sp.Fori(0, passes) as p:
                sp.wait_ge(windows_ready, p + 1)

                def step(i, u):
                    if not exists(i, u, 3):
                        return
                    s = slot(u, 3)
                    if exists(i, u, -1):
                        sp.wait_ge(e_ps_ready, done(p, i, u, -1))
                        sp.wait_ge(q_ps_ready, done(p, i, u, -1))
                    g = SLOTS * i + (u + 3)
                    sp.dma_start(edge[s][0:DIM, :],
                                 edge_tiles[bass.ds(g, 1)].rearrange("a d n -> (a d) n")
                                 ).then_inc(edge_ready[s], 16)
                    start = sp.value_load(start_i[0:1, bass.ds(g, 1)], min_val=0, max_val=LAST_WINDOW)
                    for j in range(GROUP_TILES):
                        sp.dma_start(q_diag[s][j * WINDOW:(j + 1) * WINDOW, j * DIM:(j + 1) * DIM],
                                     q_table[bass.ds(start, WINDOW), :]).then_inc(q_ready[s], 16)

                all_groups(sp, step, -3, GROUPS - 1)

            def store(i, h):
                sp.wait_ge(normed_ready, 2 * i + h + 1)
                t = CHUNK * (2 * i + h)
                sp.dma_start(out[0:112, bass.ds(t, CHUNK), :], normed[h][0:112]).then_inc(out_written[h], 16)
                sp.dma_start(out[112:NODE_PARTITIONS, bass.ds(t, CHUNK), :],
                             normed[h][112:NODE_PARTITIONS]).then_inc(out_written[h], 16)

            with sp.Fori(0, CHUNKS // 2) as i:
                for h in range(2):
                    store(i, h)
            for h in range(2):
                sp.wait_ge(out_written[h], 32 * (CHUNKS // 2))

        @block.gpsimd
        def _(pool):
            steps = [0]

            def link(instruction):
                steps[0] += 1
                instruction.then_inc(ids_made, 1)
                pool.wait_ge(ids_made, steps[0])

            for h in range(2):
                link(nc.gpsimd.memset(x_buf[h][DIM:DIM + 1, :], 1.0))
            pool.wait_ge(edges_ready, 16)
            link(nc.gpsimd.tensor_copy(dst_f[:, :], dst_sb[:, :]))
            pool.wait_ge(first_ready, 16)
            link(nc.gpsimd.tensor_copy(base_f[:, :], first_sb[:, :]))
            for s in range(SLOTS):
                link(nc.gpsimd.memset(edge[s][DIM:DIM + 1, :], 1.0))
                link(nc.gpsimd.memset(q_diag[s][:, :], 0.0))
            link(nc.gpsimd.memset(identity[:, :], 0.0))
            link(nc.gpsimd.affine_select(out=identity[:, :], in_=identity[:, :], compare_op=ALU.not_equal, fill=1.0,
                                         base=0, pattern=[[-1, P]], channel_multiplier=1))
            link(nc.gpsimd.iota(window_ids[:, :], [[1, WINDOW]], base=0, channel_multiplier=0,
                                allow_small_or_imprecise_dtypes=True))
            link(nc.gpsimd.memset(eps[:, :], 1e-5))
            nc.gpsimd.memset(acc[:, :], 0.0).then_inc(constants_ready, 1)
            pool.wait_ge(constants_ready, 1)
            pool.wait_ge(low_ready, 1)
            nc.gpsimd.partition_all_reduce(low[:, 1:2], low[:, 0:1], P, bass.bass_isa.ReduceOp.max
                                           ).then_inc(low_all_ready, 1)
            pool.wait_ge(low_all_ready, 1)
            pool.wait_ge(high_ready, 1)
            nc.gpsimd.partition_all_reduce(high[:, 1:2], high[:, 0:1], P, bass.bass_isa.ReduceOp.max
                                           ).then_inc(high_all_ready, 1)
            pool.wait_ge(high_all_ready, 1)

            passes = number_of_passes(pool)
            for h in range(2):
                pool.wait_ge(table_written[h], 32 * (CHUNKS // 2))
            with pool.Fori(0, passes) as p:
                pool.wait_ge(windows_ready, p + 1)

                def step(i, u):
                    pool.wait_ge(idx_ready, done(p, i, u))
                    if exists(i, u, -4):
                        pool.wait_ge(msg_ready, done(p, i, u, -4))
                    pool.sem_inc(gathers_begun, 1)
                    for j in range(GROUP_TILES):
                        nc.gpsimd.indirect_dma_start(
                            out=kv[u][:, j, :], out_offset=None, in_=kv_table,
                            in_offset=bass.IndirectOffsetOnAxis(ap=idx[u][:, j:j + 1], axis=0),
                        ).then_inc(kv_ready[u], 16)

                all_groups(pool, step, 0, GROUPS - 1)

            pool.wait_ge(acc_done, passes * GROUPS)
            acc_by_tile = acc[:, :].rearrange("m (p t) -> m t p", t=NODE_TILES)

            def node_chunk(i, h, again):
                if again:
                    pool.wait_ge(node_ps_ready, 2 * i + h - 1)
                if again or h:
                    pool.wait_ge(acc_tile_ready, 2 * i + h)
                pool.sem_inc(acc_tiles_begun, 1)
                nc.gpsimd.tensor_copy(acc_tile[h][:, :, :],
                                      acc_by_tile[:, bass.ds(CHUNK * (2 * i + h), CHUNK), 0:NODE_PARTITIONS]
                                      ).then_inc(acc_tile_ready, 1)

            for h in range(2):
                node_chunk(0, h, False)
            with pool.Fori(1, CHUNKS // 2) as i:
                for h in range(2):
                    node_chunk(i, h, True)

        @block.vector
        def _(dve):
            steps = [0]

            def link(instruction):
                steps[0] += 1
                instruction.then_inc(window_step, 1)
                dve.wait_ge(window_step, steps[0])

            rel_g = rel[:, :].rearrange("p (g t) -> p g t", t=GROUP_TILES)
            dst_g = dst_f[:, :].rearrange("p (g t) -> p g t", t=GROUP_TILES)
            base_g = base_f[:, :].unsqueeze(2).to_broadcast([P, GROUPS, GROUP_TILES])
            dve.wait_ge(ids_made, 4)
            link(nc.vector.tensor_tensor(rel_g, dst_g, base_g, ALU.subtract))
            nc.vector.tensor_reduce(low[:, 0:1], rel[:, :], AX.X, ALU.min, negate=True).then_inc(low_ready, 1)
            dve.wait_ge(low_all_ready, 1)
            link(nc.vector.tensor_scalar(sorted_flag[:, :], low[:, 1:2], 0.0, None, ALU.is_le))
            link(nc.vector.tensor_scalar(base_f[:, :], base_f[:, :], sorted_flag[:, 0:1], None, ALU.mult))
            link(nc.vector.tensor_tensor(rel_g, dst_g, base_g, ALU.subtract))
            nc.vector.tensor_reduce(high[:, 0:1], rel[:, :], AX.X, ALU.max).then_inc(high_ready, 1)
            link(nc.vector.tensor_copy(start_f[0:1, :], base_f[0:1, :]))
            link(nc.vector.tensor_copy(start_i[0:1, :], start_f[0:1, :]))
            dve.wait_ge(high_all_ready, 1)
            nc.vector.tensor_copy(high_i[:, :], high[:, 1:2]).then_inc(passes_ready, 1)
            dve.wait_ge(passes_ready, 1)
            dve.wait_ge(constants_ready, 1)
            dve.sem_inc(windows_ready, 1)

            passes = number_of_passes(dve)
            with dve.Fori(0, passes) as p:
                def step(i, u):
                    b = u % 2
                    if exists(i, u):
                        dve.wait_ge(kv_ready[u], 64 * slot_uses(p, i, u))
                        dve.wait_ge(q_ps_ready, done(p, i, u))
                        if exists(i, u, -1):
                            dve.wait_ge(score_done, done(p, i, u, -1))
                        nc.vector.tensor_tensor(
                            prod[:, :, :], kv[u][:, :, 0:DIM],
                            q_ps[b].rearrange("p (t d) -> p t d", d=DIM), ALU.mult).then_inc(kq_done, 1)
                    if exists(i, u, -1):
                        s, b1 = slot(u, -1), (u - 1) % 2
                        dve.wait_ge(exp_ready, done(p, i, u, -1))
                        nc.vector.tensor_tensor(
                            msg[b1][:, :, 0:DIM].rearrange("p t (h d) -> p t h d", d=HEAD_DIM),
                            kv[s][:, :, DIM:2 * DIM].rearrange("p t (h d) -> p t h d", d=HEAD_DIM),
                            msg[b1][:, :, DIM:MSG].unsqueeze(3).to_broadcast([P, GROUP_TILES, HEADS, HEAD_DIM]),
                            ALU.mult).then_inc(msg_ready, 1)
                    if exists(i, u):
                        dve.wait_ge(kq_done, done(p, i, u))
                        dve.wait_ge(e_ps_ready, done(p, i, u))
                        nc.vector.tensor_tensor(
                            prod[:, :, :], prod[:, :, :],
                            e_ps[b].rearrange("p (t d) -> p t d", d=DIM), ALU.mult).then_inc(kqe_done, 1)
                    if exists(i, u, -2):
                        g = SLOTS * i + (u - 2)
                        start = dve.value_load(start_i[0:1, bass.ds(g, 1)], min_val=0, max_val=LAST_WINDOW)
                        dve.wait_ge(sum_ps_ready, done(p, i, u, -2))
                        if exists(i, u, -3):
                            dve.wait_ge(acc_done, done(p, i, u, -3))
                        nc.vector.tensor_tensor(
                            acc[:, bass.ds(start, WINDOW)], acc[:, bass.ds(start, WINDOW)],
                            sum_ps[b], ALU.add).then_inc(acc_done, 1)
                    if exists(i, u):
                        dve.wait_ge(kqe_done, done(p, i, u))
                        nc.vector.tensor_reduce(
                            score[:, :], prod[:, :, :].rearrange("p t (h d) -> p (t h) d", d=HEAD_DIM),
                            AX.X, ALU.add).then_inc(score_done, 1)
                    if exists(i, u, 2):
                        g = SLOTS * i + (u + 2)
                        nc.vector.tensor_tensor(
                            hot[slot(u, 2)][:, :, :],
                            window_ids[:, :].unsqueeze(1).to_broadcast([P, GROUP_TILES, WINDOW]),
                            rel[:, bass.ds(GROUP_TILES * g, GROUP_TILES)].unsqueeze(2)
                            .to_broadcast([P, GROUP_TILES, WINDOW]), ALU.is_equal).then_inc(hot_ready, 1)
                    if exists(i, u):
                        dve.wait_ge(score_done, done(p, i, u))
                        if exists(i, u, -2):
                            dve.wait_ge(exp_ready, done(p, i, u, -2))
                        nc.vector.tensor_scalar(clipped[b][:, :, :].rearrange("p t h -> p (t h)"), score[:, :],
                                                -CLIP, CLIP, ALU.max, ALU.min).then_inc(clipped_ready, 1)

                all_groups(dve, step, -2, GROUPS + 1)
                dve.wait_ge(acc_done, p * GROUPS + GROUPS)
                nc.vector.tensor_scalar(window_ids[:, :], window_ids[:, :], float(WINDOW), None, ALU.add
                                        ).then_inc(window_step, 1)
                nc.vector.tensor_scalar(start_f[0:1, :], start_f[0:1, :], float(WINDOW), float(LAST_WINDOW),
                                        ALU.add, ALU.min).then_inc(window_step, 1)
                dve.wait_ge(window_step, p * 3 + (steps[0] + 2))
                nc.vector.tensor_copy(start_i[0:1, :], start_f[0:1, :]).then_inc(window_step, 1)
                dve.wait_ge(window_step, p * 3 + (steps[0] + 3))
                dve.sem_inc(windows_ready, 1)

            dve.wait_ge(residual_ready, 32)
            EPI_STEPS = 4

            def node_chunk(i, h, again):
                c = 2 * i + h
                n = NODE_PARTITIONS
                dve.wait_ge(node_ps_ready, c + 1)
                nc.vector.tensor_scalar(z[h][:, :, :], node_ps[h][:, :, DIM:MSG], 1e-6, None, ALU.add
                                        ).then_inc(node_step, 1)
                dve.wait_ge(node_step, c * EPI_STEPS + 1)
                nc.vector.reciprocal(rz[h][:, :, :], z[h][:, :, :]).then_inc(node_step, 1)
                dve.wait_ge(node_step, c * EPI_STEPS + 2)
                nc.vector.tensor_tensor(
                    attn[h][:, :, :].rearrange("p t (h d) -> p t h d", d=HEAD_DIM),
                    node_ps[h][:, :, 0:DIM].rearrange("p t (h d) -> p t h d", d=HEAD_DIM),
                    rz[h][:, :, :].unsqueeze(3).to_broadcast([n, CHUNK, HEADS, HEAD_DIM]),
                    ALU.mult).then_inc(attn_ready, 1)
                dve.wait_ge(attn_ready, c + 1)
                if again:
                    dve.wait_ge(normed_ready, c - 1)
                nc.vector.tensor_tensor(y[h][:, :, :], attn[h][:, :, :], x_res[:, bass.ds(CHUNK * c, CHUNK), :],
                                        ALU.add).then_inc(y_ready, 1)
                dve.wait_ge(y_ready, c + 1)
                for t in range(CHUNK):
                    last = nc.vector.bn_stats(stats[h][:, t, :], y[h][:, t, :])
                last.then_inc(node_step, 1)
                dve.wait_ge(node_step, c * EPI_STEPS + 3)
                dve.sem_inc(aggregates_begun, 1)
                for t in range(CHUNK):
                    last = nc.vector.bn_aggr(mean_var[h][:, t, :], stats[h][:, t, :])
                last.then_inc(var_ready, 1)
                dve.wait_ge(std_ready, c + 1)
                nc.vector.reciprocal(rstd[h][:, :], std[h][:, :]).then_inc(node_step, 1)
                dve.wait_ge(node_step, c * EPI_STEPS + 4)
                nc.vector.scalar_tensor_tensor(out=shift[h][:, :], in0=mean_var[h][:, :, 0], scalar=-1.0,
                                               in1=rstd[h][:, :], op0=ALU.mult, op1=ALU.mult
                                               ).then_inc(shift_ready, 1)

            for h in range(2):
                node_chunk(0, h, False)
            with dve.Fori(1, CHUNKS // 2) as i:
                for h in range(2):
                    node_chunk(i, h, True)

        @block.scalar
        def _(act):
            def stage(i, h, again):
                for t in range(CHUNK):
                    act.wait_ge(table_tile_ready, CHUNK * (2 * i + h) + (t + 1))
                    if t == 0 and again:
                        act.wait_ge(table_written[h], 32 * i)
                    nc.scalar.copy(kv_stage[:, h, t, :], table_ps[t][:, 0:2 * DIM])
                    nc.scalar.copy(q_stage[:, h, t, :], table_ps[t][:, 2 * DIM:3 * DIM]
                                   ).then_inc(table_tile_staged, 1)

            for h in range(2):
                stage(0, h, False)
            with act.Fori(1, CHUNKS // 2) as i:
                for h in range(2):
                    stage(i, h, True)

            passes = number_of_passes(act)
            act.wait_ge(src_ready, 16)
            with act.Fori(0, passes) as p:
                act.wait_ge(windows_ready, p + 1)

                def step(i, u):
                    b = u % 2
                    if exists(i, u, 3):
                        s = slot(u, 3)
                        if exists(i, u, -1):
                            act.wait_ge(kv_ready[s], 64 * slot_uses(p, i, u, -1))
                        nc.scalar.copy(idx[s][:, :],
                                       src_sb[:, bass.ds(GROUP_TILES * (SLOTS * i + (u + 3)), GROUP_TILES)]
                                       ).then_inc(idx_ready, 1)
                    if exists(i, u):
                        act.wait_ge(clipped_ready, done(p, i, u))
                        if exists(i, u, -2):
                            act.wait_ge(sum_ps_ready, done(p, i, u, -2))
                        nc.scalar.activation(msg[b][:, :, DIM:MSG], clipped[b][:, :, :], ACT.Exp,
                                             scale=SCALE).then_inc(exp_ready, 1)
                    if exists(i, u, 2):
                        act.wait_ge(hot_ps_ready, done(p, i, u, 2))
                        if exists(i, u):
                            act.wait_ge(q_ps_ready, done(p, i, u))
                        nc.scalar.copy(hot_t[b][:, :], hot_ps[b]).then_inc(hot_t_ready, 1)

                all_groups(act, step, -3, GROUPS - 1)

            def node_chunk(i, h, again):
                c = 2 * i + h
                act.wait_ge(var_ready, c + 1)
                nc.scalar.activation(std[h][:, :], mean_var[h][:, :, 1], ACT.Sqrt,
                                     bias=eps[0:NODE_PARTITIONS, 0:1]).then_inc(std_ready, 1)
                act.wait_ge(shift_ready, c + 1)
                if again:
                    act.wait_ge(out_written[h], 32 * i)
                for t in range(CHUNK):
                    last = nc.scalar.activation(normed[h][:, t, :], y[h][:, t, :], ACT.Identity,
                                                bias=shift[h][:, t:t + 1], scale=rstd[h][:, t:t + 1])
                last.then_inc(normed_ready, 1)

            for h in range(2):
                node_chunk(0, h, False)
            with act.Fori(1, CHUNKS // 2) as i:
                for h in range(2):
                    node_chunk(i, h, True)

        @block.tensor
        def _(pe):
            pe.wait_ge(weights_ready, 16)
            pe.wait_ge(ids_made, 2)

            def table_chunk(i, h, again):
                pe.wait_ge(x_ready[h], 16 * (i + 1))
                for t in range(CHUNK):
                    if again or h:
                        pe.wait_ge(table_tile_staged, CHUNK * (2 * i + h) + (t + 1 - CHUNK))
                    nc.tensor.matmul(table_ps[t], x_buf[h][:, t * P:(t + 1) * P], w_kvq,
                                     start=True, stop=True).then_inc(table_tile_ready, 1)

            for h in range(2):
                table_chunk(0, h, False)
            with pe.Fori(1, CHUNKS // 2) as i:
                for h in range(2):
                    table_chunk(i, h, True)

            passes = number_of_passes(pe)
            pe.wait_ge(constants_ready, 1)
            pe.wait_ge(table_tile_staged, NODE_TILES)
            with pe.Fori(0, passes) as p:
                pe.wait_ge(windows_ready, p + 1)

                def step(i, u):
                    s1, b1 = slot(u, 1), (u + 1) % 2
                    if exists(i, u, 1):
                        pe.wait_ge(edge_ready[s1], 16 * slot_uses(p, i, u, 1))
                        if exists(i, u, -1):
                            pe.wait_ge(kqe_done, done(p, i, u, -1))
                        for j in range(GROUP_TILES):
                            last = nc.tensor.matmul(e_ps[b1][:, j * DIM:(j + 1) * DIM],
                                                    edge[s1][:, j * TILE:(j + 1) * TILE], w_edge,
                                                    start=True, stop=True)
                        last.then_inc(e_ps_ready, 1)
                        pe.wait_ge(hot_t_ready, done(p, i, u, 1))
                        pe.wait_ge(q_ready[s1], 64 * slot_uses(p, i, u, 1))
                        if exists(i, u, -1):
                            pe.wait_ge(kq_done, done(p, i, u, -1))
                        nc.tensor.matmul(q_ps[b1], hot_t[b1][:, :], q_diag[s1][:, :],
                                         start=True, stop=True).then_inc(q_ps_ready, 1)
                    if exists(i, u, -1):
                        pe.wait_ge(msg_ready, done(p, i, u, -1))
                        if exists(i, u, -3):
                            pe.wait_ge(acc_done, done(p, i, u, -3))
                        for j in range(GROUP_TILES):
                            last = nc.tensor.matmul(sum_ps[b1], msg[b1][:, j, :], hot[slot(u, -1)][:, j, :],
                                                    start=(j == 0), stop=(j == GROUP_TILES - 1))
                        last.then_inc(sum_ps_ready, 1)
                    if exists(i, u, 2):
                        pe.wait_ge(hot_ready, done(p, i, u, 2))
                        if exists(i, u):
                            pe.wait_ge(hot_t_ready, done(p, i, u))
                        nc.tensor.transpose(hot_ps[u % 2], hot[slot(u, 2)][:, :, :].rearrange("p t n -> p (t n)"),
                                            identity[:, :]).then_inc(hot_ps_ready, 1)

                all_groups(pe, step, -2, GROUPS)

            def node_chunk(i, h, again):
                c = 2 * i + h
                pe.wait_ge(acc_tile_ready, c + 1)
                if again:
                    pe.wait_ge(attn_ready, c - 1)
                for t in range(CHUNK):
                    last = nc.tensor.transpose(node_ps[h][:, t, 0:MSG], acc_tile[h][:, t, :],
                                               identity[0:MSG, 0:MSG])
                last.then_inc(node_ps_ready, 1)

            for h in range(2):
                node_chunk(0, h, False)
            with pe.Fori(1, CHUNKS // 2) as i:
                for h in range(2):
                    node_chunk(i, h, True)


def kernel(x, src, dst, edge_attr_96, L0_gnn_Wq, L0_gnn_bq, L0_gnn_Wk, L0_gnn_bk, L0_gnn_We, L0_gnn_be,
           L0_gnn_Wv, L0_gnn_bv):
    import numpy as np
    import concourse.bacc as bacc
    from concourse.bass_utils import run_bass_kernel_spmd

    x, src, dst, edges = (np.asarray(a) for a in (x, src, dst, edge_attr_96))
    pad_edges = TILES * TILE - EDGES
    x_pad = np.concatenate([x, np.zeros((NODES_PAD - NODES, DIM), x.dtype)])
    x_tiles = x_pad.reshape(P, CHUNKS, CHUNK, DIM).transpose(1, 3, 2, 0).reshape(CHUNKS, DIM, CHUNK * P)
    edges_pad = np.concatenate([edges, np.zeros((pad_edges, DIM), edges.dtype)])
    edge_tiles = edges_pad.reshape(GROUPS, GROUP, DIM).transpose(0, 2, 1)
    src_pad = np.concatenate([src, np.zeros(pad_edges, src.dtype)])
    dst_pad = np.concatenate([dst, np.full(pad_edges, NODES, dst.dtype)])
    weights = np.concatenate([
        np.concatenate([np.asarray(w) for w in (L0_gnn_Wk, L0_gnn_Wv, L0_gnn_Wq, L0_gnn_We)], axis=1),
        np.concatenate([np.asarray(b) for b in (L0_gnn_bk, L0_gnn_bv, L0_gnn_bq, L0_gnn_be)])[None, :]])
    arrays = {
        "x_tiles": x_tiles,
        "x_rows": x.reshape(NODE_PARTITIONS, NODE_TILES, DIM),
        "edge_tiles": edge_tiles,
        "src": src_pad.reshape(TILES, TILE).T,
        "dst": dst_pad.reshape(TILES, TILE).T,
        "first_dst": dst_pad[::GROUP][None, :],
        "weights": weights,
    }
    arrays = {name: np.ascontiguousarray(a) for name, a in arrays.items()}
    nc = bacc.Bacc("TRN2", target_bir_lowering=False, num_devices=1)
    args = [nc.dram_tensor(f"in_{name}", a.shape, mybir.dt.from_np(a.dtype), kind="ExternalInput").ap()
            for name, a in arrays.items()]
    out = nc.dram_tensor("out_nodes", (NODE_PARTITIONS, NODE_TILES, DIM), mybir.dt.float32,
                         kind="ExternalOutput").ap()
    gnn_resnorm(nc, *args, out)
    r = run_bass_kernel_spmd(nc, [{f"in_{name}": a for name, a in arrays.items()}], core_ids=[0])
    return r.results[0]["out_nodes"].reshape(NODES, DIM)
```

```python
import concourse.bass as bass
from concourse import mybir
from contextlib import ExitStack

NODES = 6250
EDGES = 206250
DIM = 96
HEADS = 8
HEAD_DIM = DIM // HEADS
MSG = DIM + HEADS

P = 128
TILE = 128
TILES = -(-EDGES // TILE)
GROUP_TILES = 4
GROUP = GROUP_TILES * TILE
GROUPS = TILES // GROUP_TILES
SLOTS = 4
WINDOW = 32
LOOP_ITERATIONS = GROUPS // SLOTS
SLOT_GROUPS = [len(range(s, GROUPS, SLOTS)) for s in range(SLOTS)]

NODE_TILES = 50
NODE_PARTITIONS = NODES // NODE_TILES
NODES_PAD = P * NODE_TILES
CHUNK = 5
CHUNKS = NODE_TILES // CHUNK
LAST_WINDOW = -(-NODES // WINDOW) * WINDOW
Q_PARTS = 3
CLIP = 5.0 * HEAD_DIM ** 0.5
SCALE = HEAD_DIM ** -0.5
assert TILES % GROUP_TILES == 0 and NODES % NODE_TILES == 0 and LAST_WINDOW + WINDOW <= NODES_PAD


def gnn_resnorm(nc, x_tiles, x_rows, edge_tiles, src, dst, first_dst, weights, out):
    fp32 = mybir.dt.float32
    int32 = mybir.dt.int32
    bf16 = mybir.dt.bfloat16
    ALU = mybir.AluOpType
    ACT = mybir.ActivationFunctionType
    AX = mybir.AxisListType

    kv_table = nc.dram_tensor("kv_table", [NODES_PAD, 2 * DIM], fp32).ap()
    q_table = nc.dram_tensor("q_table", [NODES_PAD, Q_PARTS * DIM], bf16).ap()
    kv_table_tiles = kv_table.rearrange("(p t) d -> p t d", t=NODE_TILES)
    q_table_tiles = q_table.rearrange("(p t) d -> p t d", t=NODE_TILES)

    ctx = ExitStack()
    with ctx:
        def sb(name, shape, dt=fp32):
            return ctx.enter_context(nc.sbuf_tensor(name, shape, dt))

        def sem(name):
            return ctx.enter_context(nc.semaphore(name))

        w_all = sb("w_all", [DIM + 1, 4 * DIM])
        w_kvq = w_all[:, 0:3 * DIM]
        w_edge = w_all[:, 3 * DIM:4 * DIM]
        identity = sb("identity", [P, P])
        identity_bf = sb("identity_bf", [P, P], bf16)
        window_ids = sb("window_ids", [P, WINDOW])
        eps = sb("eps", [P, 1])
        src_sb = sb("src_sb", [P, TILES], int32)
        dst_sb = sb("dst_sb", [P, TILES], int32)
        first_sb = sb("first_sb", [P, GROUPS], int32)
        base_f = sb("base_f", [P, GROUPS])
        rel = sb("rel", [P, TILES])
        start_f = sb("start_f", [1, GROUPS])
        start_i = sb("start_i", [1, GROUPS], int32)
        low = sb("low", [P, 2])
        sorted_flag = sb("sorted_flag", [P, 1])
        high = sb("high", [P, 2])
        high_i = sb("high_i", [P, 1], int32)

        x_buf = [sb(f"x_buf{h}", [DIM + 1, CHUNK * P]) for h in range(2)]
        kv_stage = sb("kv_stage", [P, 2, CHUNK, 2 * DIM])
        q_parts = sb("q_parts", [P, NODE_TILES, Q_PARTS, DIM], bf16)
        node_rows = sb("node_rows", [P, NODE_TILES, DIM])
        q_rest = node_rows

        idx = [sb(f"idx{s}", [P, GROUP_TILES], int32) for s in range(SLOTS)]
        kv = [sb(f"kv{s}", [P, GROUP_TILES, 2 * DIM]) for s in range(SLOTS)]
        edge = [sb(f"edge{s}", [DIM + 1, GROUP]) for s in range(SLOTS)]
        q_diag = [sb(f"q_diag{s}", [P, GROUP_TILES, Q_PARTS, DIM], bf16) for s in range(SLOTS)]
        hot = [sb(f"hot{s}", [P, GROUP_TILES, WINDOW]) for s in range(SLOTS)]
        hot_bf = [sb(f"hot_bf{b}", [P, GROUP_TILES, WINDOW], bf16) for b in range(2)]
        hot_t = [sb(f"hot_t{b}", [P, TILE], bf16) for b in range(2)]
        prod = sb("prod", [P, GROUP_TILES, DIM])
        score = sb("score", [P, GROUP_TILES * HEADS])
        clipped = [sb(f"clipped{b}", [P, GROUP_TILES, HEADS]) for b in range(2)]
        msg = [sb(f"msg{b}", [P, GROUP_TILES, MSG]) for b in range(2)]
        acc = sb("acc", [MSG, NODES_PAD])

        x_res = node_rows[0:NODE_PARTITIONS]
        z = [sb(f"z{h}", [NODE_PARTITIONS, CHUNK, HEADS]) for h in range(2)]
        rz = [sb(f"rz{h}", [NODE_PARTITIONS, CHUNK, HEADS]) for h in range(2)]
        attn = [sb(f"attn{h}", [NODE_PARTITIONS, CHUNK, DIM]) for h in range(2)]
        y = sb("y", [NODE_PARTITIONS, NODE_TILES, DIM])
        stats = [sb(f"stats{h}", [NODE_PARTITIONS, CHUNK, 6]) for h in range(2)]
        mean_var = [sb(f"mean_var{h}", [NODE_PARTITIONS, CHUNK, 2]) for h in range(2)]
        std = [sb(f"std{h}", [NODE_PARTITIONS, CHUNK]) for h in range(2)]
        rstd = [sb(f"rstd{h}", [NODE_PARTITIONS, CHUNK]) for h in range(2)]
        shift = [sb(f"shift{h}", [NODE_PARTITIONS, CHUNK]) for h in range(2)]

        banks = ctx.enter_context(nc.psum_tensor("banks", [P, 8, 512], fp32))
        hot_ps = [banks[:, b, 0:TILE] for b in range(2)]
        e_ps = [banks[:, 2 + b, 0:GROUP_TILES * DIM] for b in range(2)]
        q_ps = [banks[:, 4 + b, 0:GROUP_TILES * DIM] for b in range(2)]
        sum_ps = [banks[0:MSG, 6 + b, 0:WINDOW] for b in range(2)]
        table_ps = [banks[:, t, 0:3 * DIM] for t in range(CHUNK)]
        node_ps = [banks[0:NODE_PARTITIONS, 4 * h:4 * h + 4, :].rearrange("p a b -> p (a b)")[:, 0:CHUNK * P]
                   .rearrange("p (t d) -> p t d", d=P) for h in range(2)]

        weights_ready = sem("weights_ready")
        edges_ready = sem("edges_ready")
        first_ready = sem("first_ready")
        src_ready = sem("src_ready")
        residual_ready = sem("residual_ready")
        constants_ready = sem("constants_ready")
        x_ready = [sem(f"x_ready{h}") for h in range(2)]
        table_ps_ready = sem("table_ps_ready")
        table_staged = sem("table_staged")
        kv_written = [sem(f"kv_written{h}") for h in range(2)]
        q_middle_ready = sem("q_middle_ready")
        q_high_ready = sem("q_high_ready")
        q_rest_ready = sem("q_rest_ready")
        q_low_ready = sem("q_low_ready")
        q_written = sem("q_written")
        ids_made = sem("ids_made")
        window_step = sem("window_step")
        low_ready = sem("low_ready")
        low_all_ready = sem("low_all_ready")
        high_ready = sem("high_ready")
        high_all_ready = sem("high_all_ready")
        passes_ready = sem("passes_ready")
        windows_ready = sem("windows_ready")

        idx_ready = sem("idx_ready")
        kv_ready = [sem(f"kv_ready{s}") for s in range(SLOTS)]
        edge_ready = [sem(f"edge_ready{s}") for s in range(SLOTS)]
        q_ready = [sem(f"q_ready{s}") for s in range(SLOTS)]
        hot_ready = sem("hot_ready")
        identity_ready = sem("identity_ready")
        hot_bf_ready = sem("hot_bf_ready")
        hot_ps_ready = sem("hot_ps_ready")
        hot_t_ready = sem("hot_t_ready")
        e_ps_ready = sem("e_ps_ready")
        q_ps_ready = sem("q_ps_ready")
        kq_done = sem("kq_done")
        kqe_done = sem("kqe_done")
        score_done = sem("score_done")
        clipped_ready = sem("clipped_ready")
        exp_ready = sem("exp_ready")
        msg_ready = sem("msg_ready")
        sum_ps_ready = sem("sum_ps_ready")
        acc_done = sem("acc_done")

        pass_gathered = sem("pass_gathered")
        aggregates_begun = sem("aggregates_begun")
        node_ps_ready = sem("node_ps_ready")
        z_ready = sem("z_ready")
        rz_ready = sem("rz_ready")
        stats_ready = sem("stats_ready")
        rstd_ready = sem("rstd_ready")
        attn_ready = sem("attn_ready")
        var_ready = sem("var_ready")
        std_ready = sem("std_ready")
        shift_ready = sem("shift_ready")
        normed_ready = sem("normed_ready")
        y_ready = sem("y_ready")
        out_written = sem("out_written")

        def exists(i, u, k=0):
            return not isinstance(i, int) or 0 <= SLOTS * i + u + k < GROUPS

        def done(p, i, u, k=0):
            return p * GROUPS + i * SLOTS + (u + k + 1)

        def slot(u, k=0):
            return (u + k) % SLOTS

        def slot_uses(p, i, u, k=0):
            return p * SLOT_GROUPS[slot(u, k)] + i + ((u + k) // SLOTS + 1)

        def all_groups(eng, step, first, last):
            for g in range(first, SLOTS):
                step(g // SLOTS, g % SLOTS)
            with eng.Fori(1, LOOP_ITERATIONS) as i:
                for u in range(SLOTS):
                    step(i, u)
            for g in range(SLOTS * LOOP_ITERATIONS, last + 1):
                step(g // SLOTS, g % SLOTS)

        def chunk_exists(i, h, k=0):
            return not isinstance(i, int) or 0 <= 2 * i + h + k < CHUNKS

        def all_chunks(eng, step, first, last):
            for c in range(first, 2):
                step(c // 2, c % 2)
            with eng.Fori(1, CHUNKS // 2 - 1) as i:
                for h in range(2):
                    step(i, h)
            for c in range(CHUNKS - 2, last + 1):
                step(c // 2, c % 2)

        def number_of_passes(eng):
            eng.wait_ge(passes_ready, 1)
            greatest = eng.value_load(high_i[0:1, 0:1], min_val=0, max_val=LAST_WINDOW - 1)
            return eng.snap(greatest // WINDOW + 1)

        block = ctx.enter_context(nc.Block())

        @block.sync
        def _(sp):
            sp.dma_start(w_all[0:DIM, :], weights[0:DIM, :]).then_inc(weights_ready, 16)
            sp.dma_start(w_all[DIM:DIM + 1, :], weights[DIM:DIM + 1, :]).then_inc(weights_ready, 16)
            for h in range(2):
                sp.dma_start(x_buf[h][0:DIM, :], x_tiles[h]).then_inc(x_ready[h], 16)
            sp.dma_start(dst_sb[:, :], dst).then_inc(edges_ready, 16)
            sp.dma_start(first_sb[:, :], first_dst.to_broadcast([P, GROUPS])).then_inc(first_ready, 16)
            sp.dma_start(src_sb[:, :], src).then_inc(src_ready, 16)

            def load_x(i, h):
                sp.wait_ge(table_ps_ready, CHUNK * (2 * i + h + 1))
                sp.dma_start(x_buf[h][0:DIM, :],
                             x_tiles[bass.ds(2 * i + h + 2, 1)].rearrange("a d n -> (a d) n")
                             ).then_inc(x_ready[h], 16)

            def write_kv(i, h):
                sp.wait_ge(table_staged, CHUNK * (2 * i + h + 1))
                sp.dma_start(kv_table_tiles[:, bass.ds(CHUNK * (2 * i + h), CHUNK), :],
                             kv_stage[:, h, :, :]).then_inc(kv_written[h], 16)

            def write_q(i):
                sp.wait_ge(q_low_ready, i + 1)
                sp.dma_start(q_table_tiles[:, bass.ds(2 * CHUNK * i, 2 * CHUNK), :],
                             q_parts[:, bass.ds(2 * CHUNK * i, 2 * CHUNK), :, :].rearrange("p t k d -> p t (k d)")
                             ).then_inc(q_written, 16)

            for h in range(2):
                load_x(0, h)
                write_kv(0, h)
            with sp.Fori(1, CHUNKS // 2 - 1) as i:
                for h in range(2):
                    load_x(i, h)
                    write_kv(i, h)
                write_q(i - 1)
            for h in range(2):
                write_kv(CHUNKS // 2 - 1, h)
            for i in (CHUNKS // 2 - 2, CHUNKS // 2 - 1):
                write_q(i)

            passes = number_of_passes(sp)
            sp.wait_ge(q_written, 16 * (CHUNKS // 2))
            sp.wait_ge(constants_ready, 1)
            with sp.Fori(0, passes) as p:
                sp.wait_ge(windows_ready, 2 * p + 1)

                def step(i, u):
                    if not exists(i, u, 3):
                        return
                    s = slot(u, 3)
                    if exists(i, u, -1):
                        sp.wait_ge(e_ps_ready, done(p, i, u, -1))
                        sp.wait_ge(q_ps_ready, done(p, i, u, -1))
                    g = SLOTS * i + (u + 3)
                    sp.dma_start(edge[s][0:DIM, :],
                                 edge_tiles[bass.ds(g, 1)].rearrange("a d n -> (a d) n")
                                 ).then_inc(edge_ready[s], 16)
                    start = sp.value_load(start_i[0:1, bass.ds(g, 1)], min_val=0, max_val=LAST_WINDOW)
                    for j in range(GROUP_TILES):
                        sp.dma_start(q_diag[s][j * WINDOW:(j + 1) * WINDOW, j, :, :].rearrange("p k d -> p (k d)"),
                                     q_table[bass.ds(start, WINDOW), :]).then_inc(q_ready[s], 16)

                all_groups(sp, step, -3, GROUPS - 1)

            sp.dma_start(x_res[0:112], x_rows[0:112]).then_inc(residual_ready, 16)
            sp.dma_start(x_res[112:NODE_PARTITIONS], x_rows[112:NODE_PARTITIONS]).then_inc(residual_ready, 16)

            def store(i, h):
                sp.wait_ge(normed_ready, 2 * i + h + 1)
                t = bass.ds(CHUNK * (2 * i + h), CHUNK)
                sp.dma_start(out[0:112, t, :], y[0:112, t, :]).then_inc(out_written, 16)
                sp.dma_start(out[112:NODE_PARTITIONS, t, :], y[112:NODE_PARTITIONS, t, :]
                             ).then_inc(out_written, 16)

            all_chunks(sp, store, 0, CHUNKS - 1)
            sp.wait_ge(out_written, 32 * CHUNKS)

        @block.gpsimd
        def _(pool):
            steps = [0]

            def link(instruction):
                steps[0] += 1
                instruction.then_inc(ids_made, 1)
                pool.wait_ge(ids_made, steps[0])

            for h in range(2):
                link(nc.gpsimd.memset(x_buf[h][DIM:DIM + 1, :], 1.0))
            link(nc.gpsimd.memset(identity[:, :], 0.0))
            link(nc.gpsimd.affine_select(out=identity[:, :], in_=identity[:, :], compare_op=ALU.not_equal, fill=1.0,
                                         base=0, pattern=[[-1, P]], channel_multiplier=1))
            link(nc.gpsimd.iota(window_ids[:, :], [[1, WINDOW]], base=0, channel_multiplier=0,
                                allow_small_or_imprecise_dtypes=True))
            link(nc.gpsimd.memset(eps[:, :], 1e-5))
            pool.wait_ge(low_ready, 1)
            nc.gpsimd.partition_all_reduce(low[:, 1:2], low[:, 0:1], P, bass.bass_isa.ReduceOp.max
                                           ).then_inc(low_all_ready, 1)
            pool.wait_ge(low_all_ready, 1)
            pool.wait_ge(high_ready, 1)
            nc.gpsimd.partition_all_reduce(high[:, 1:2], high[:, 0:1], P, bass.bass_isa.ReduceOp.max
                                           ).then_inc(high_all_ready, 1)
            pool.wait_ge(high_all_ready, 1)

            for s in range(SLOTS):
                link(nc.gpsimd.memset(edge[s][DIM:DIM + 1, :], 1.0))
                link(nc.gpsimd.memset(q_diag[s][:, :, :, :], 0.0))
            pool.sem_inc(constants_ready, 1)

            passes = number_of_passes(pool)
            for h in range(2):
                pool.wait_ge(kv_written[h], 16 * (CHUNKS // 2))
            group_count = pool.alloc_register("group_count")
            pool.reg_mov(group_count, 1)
            with pool.Fori(0, passes) as p:
                pool.wait_ge(windows_ready, 2 * p + 1)

                def step(i, u):
                    pool.wait_ge(idx_ready, group_count)
                    if exists(i, u, -4):
                        pool.wait_ge(msg_ready, done(p, i, u, -4))
                    pool.reg_add(group_count, group_count, 1)
                    for j in range(GROUP_TILES):
                        nc.gpsimd.indirect_dma_start(
                            out=kv[u][:, j, :], out_offset=None, in_=kv_table,
                            in_offset=bass.IndirectOffsetOnAxis(ap=idx[u][:, j:j + 1], axis=0),
                        ).then_inc(kv_ready[u], 16)

                all_groups(pool, step, 0, GROUPS - 1)
                pool.wait_ge(acc_done, p * GROUPS + GROUPS)
                pool.sem_inc(pass_gathered, 1)
                nc.gpsimd.inc_swdge_sem(kv_ready, [64 * n for n in SLOT_GROUPS], mode="sub")
                pool.sem_inc(windows_ready, 1)

            pool.wait_ge(residual_ready, 32)

            def node_step(i, h):
                c = 2 * i + h
                pool.wait_ge(attn_ready, c + 1)
                t = bass.ds(CHUNK * c, CHUNK)
                nc.gpsimd.tensor_tensor(y[:, t, :], attn[h][:, :, :], x_res[:, t, :],
                                        ALU.add).then_inc(y_ready, 1)

            all_chunks(pool, node_step, 0, CHUNKS - 1)

        @block.vector
        def _(dve):
            nc.vector.memset(acc[:, :], 0.0)
            steps = [0]

            def link(instruction):
                steps[0] += 1
                instruction.then_inc(window_step, 1)
                dve.wait_ge(window_step, steps[0])

            rel_g = rel[:, :].rearrange("p (g t) -> p g t", t=GROUP_TILES)
            dst_g = dst_sb[:, :].rearrange("p (g t) -> p g t", t=GROUP_TILES)
            dve.wait_ge(edges_ready, 16)
            dve.wait_ge(first_ready, 16)
            link(nc.vector.tensor_tensor(rel_g, dst_g, first_sb[:, :].unsqueeze(2)
                                         .to_broadcast([P, GROUPS, GROUP_TILES]), ALU.subtract))
            nc.vector.tensor_reduce(low[:, 0:1], rel[:, :], AX.X, ALU.min, negate=True).then_inc(low_ready, 1)
            dve.wait_ge(low_all_ready, 1)
            link(nc.vector.tensor_scalar(sorted_flag[:, :], low[:, 1:2], 0.0, None, ALU.is_le))
            link(nc.vector.tensor_scalar(base_f[:, :], first_sb[:, :], sorted_flag[:, 0:1], None, ALU.mult))
            link(nc.vector.tensor_tensor(rel_g, dst_g, base_f[:, :].unsqueeze(2)
                                         .to_broadcast([P, GROUPS, GROUP_TILES]), ALU.subtract))
            nc.vector.tensor_reduce(high[:, 0:1], rel[:, :], AX.X, ALU.max).then_inc(high_ready, 1)
            link(nc.vector.tensor_copy(start_f[0:1, :], base_f[0:1, :]))
            link(nc.vector.tensor_copy(start_i[0:1, :], start_f[0:1, :]))
            dve.wait_ge(high_all_ready, 1)
            nc.vector.tensor_copy(high_i[:, :], high[:, 1:2]).then_inc(passes_ready, 1)
            dve.wait_ge(passes_ready, 1)
            dve.sem_inc(windows_ready, 1)

            with dve.Fori(0, CHUNKS // 2) as i:
                t = bass.ds(2 * CHUNK * i, 2 * CHUNK)
                dve.wait_ge(q_high_ready, i + 1)
                nc.vector.tensor_tensor(q_rest[:, t, :], q_rest[:, t, :], q_parts[:, t, 0, :], ALU.subtract
                                        ).then_inc(q_rest_ready, 1)
                dve.wait_ge(q_middle_ready, i + 1)
                nc.vector.tensor_tensor(q_parts[:, t, 2, :], q_rest[:, t, :], q_parts[:, t, 1, :],
                                        ALU.subtract).then_inc(q_low_ready, 1)
            dve.wait_ge(constants_ready, 1)
            nc.vector.tensor_copy(identity_bf[:, :], identity[:, :]).then_inc(identity_ready, 1)

            passes = number_of_passes(dve)
            with dve.Fori(0, passes) as p:
                dve.wait_ge(windows_ready, 2 * p + 1)

                def step(i, u):
                    b = u % 2
                    if exists(i, u, 2):
                        if exists(i, u):
                            dve.wait_ge(hot_ps_ready, done(p, i, u))
                        g = SLOTS * i + (u + 2)
                        nc.vector.tensor_tensor(
                            hot_bf[b][:, :, :],
                            window_ids[:, :].unsqueeze(1).to_broadcast([P, GROUP_TILES, WINDOW]),
                            rel[:, bass.ds(GROUP_TILES * g, GROUP_TILES)].unsqueeze(2)
                            .to_broadcast([P, GROUP_TILES, WINDOW]), ALU.is_equal).then_inc(hot_bf_ready, 1)
                        if exists(i, u, -2):
                            dve.wait_ge(sum_ps_ready, done(p, i, u, -2))
                        nc.vector.tensor_tensor(
                            hot[slot(u, 2)][:, :, :],
                            window_ids[:, :].unsqueeze(1).to_broadcast([P, GROUP_TILES, WINDOW]),
                            rel[:, bass.ds(GROUP_TILES * g, GROUP_TILES)].unsqueeze(2)
                            .to_broadcast([P, GROUP_TILES, WINDOW]), ALU.is_equal).then_inc(hot_ready, 1)
                    if exists(i, u, -1):
                        s, b1 = slot(u, -1), (u - 1) % 2
                        dve.wait_ge(exp_ready, done(p, i, u, -1))
                        nc.vector.tensor_tensor(
                            msg[b1][:, :, 0:DIM].rearrange("p t (h d) -> p t h d", d=HEAD_DIM),
                            kv[s][:, :, DIM:2 * DIM].rearrange("p t (h d) -> p t h d", d=HEAD_DIM),
                            msg[b1][:, :, DIM:MSG].unsqueeze(3).to_broadcast([P, GROUP_TILES, HEADS, HEAD_DIM]),
                            ALU.mult).then_inc(msg_ready, 1)
                    if exists(i, u):
                        dve.wait_ge(kv_ready[u], 64 * slot_uses(0, i, u))
                        dve.wait_ge(q_ps_ready, done(p, i, u))
                        if exists(i, u, -1):
                            dve.wait_ge(score_done, done(p, i, u, -1))
                        nc.vector.tensor_tensor(
                            prod[:, :, :], kv[u][:, :, 0:DIM],
                            q_ps[b].rearrange("p (t d) -> p t d", d=DIM), ALU.mult).then_inc(kq_done, 1)
                    if exists(i, u):
                        dve.wait_ge(kq_done, done(p, i, u))
                        dve.wait_ge(e_ps_ready, done(p, i, u))
                        nc.vector.tensor_tensor(
                            prod[:, :, :], prod[:, :, :],
                            e_ps[b].rearrange("p (t d) -> p t d", d=DIM), ALU.mult).then_inc(kqe_done, 1)
                    if exists(i, u, -2):
                        g = SLOTS * i + (u - 2)
                        start = dve.value_load(start_i[0:1, bass.ds(g, 1)], min_val=0, max_val=LAST_WINDOW)
                        dve.wait_ge(sum_ps_ready, done(p, i, u, -2))
                        if exists(i, u, -3):
                            dve.wait_ge(acc_done, done(p, i, u, -3))
                        nc.vector.tensor_tensor(
                            acc[:, bass.ds(start, WINDOW)], acc[:, bass.ds(start, WINDOW)],
                            sum_ps[b], ALU.add).then_inc(acc_done, 1)
                    if exists(i, u):
                        dve.wait_ge(kqe_done, done(p, i, u))
                        nc.vector.tensor_reduce(
                            score[:, :], prod[:, :, :].rearrange("p t (h d) -> p (t h) d", d=HEAD_DIM),
                            AX.X, ALU.add).then_inc(score_done, 1)
                    if exists(i, u):
                        dve.wait_ge(score_done, done(p, i, u))
                        if exists(i, u, -2):
                            dve.wait_ge(exp_ready, done(p, i, u, -2))
                        nc.vector.tensor_scalar(clipped[b][:, :, :].rearrange("p t h -> p (t h)"), score[:, :],
                                                -CLIP, CLIP, ALU.max, ALU.min).then_inc(clipped_ready, 1)

                all_groups(dve, step, -2, GROUPS + 1)
                dve.wait_ge(acc_done, p * GROUPS + GROUPS)
                nc.vector.tensor_scalar(window_ids[:, :], window_ids[:, :], float(WINDOW), None, ALU.add
                                        ).then_inc(window_step, 1)
                nc.vector.tensor_scalar(start_f[0:1, :], start_f[0:1, :], float(WINDOW), float(LAST_WINDOW),
                                        ALU.add, ALU.min).then_inc(window_step, 1)
                dve.wait_ge(window_step, p * 3 + (steps[0] + 2))
                nc.vector.tensor_copy(start_i[0:1, :], start_f[0:1, :]).then_inc(window_step, 1)
                dve.wait_ge(window_step, p * 3 + (steps[0] + 3))
                dve.sem_inc(windows_ready, 1)

            n = NODE_PARTITIONS

            def node_step(i, h):
                c = 2 * i + h
                h1 = 1 - h
                if chunk_exists(i, h, 1):
                    dve.wait_ge(node_ps_ready, c + 2)
                    nc.vector.tensor_scalar(z[h1][:, :, :], node_ps[h1][:, :, DIM:MSG], 1e-6, None, ALU.add
                                            ).then_inc(z_ready, 1)
                if chunk_exists(i, h, -1):
                    dve.wait_ge(std_ready, c)
                    nc.vector.reciprocal(rstd[h1][:, :], std[h1][:, :]).then_inc(rstd_ready, 1)
                if chunk_exists(i, h, 1):
                    dve.wait_ge(z_ready, c + 2)
                    nc.vector.reciprocal(rz[h1][:, :, :], z[h1][:, :, :]).then_inc(rz_ready, 1)
                if chunk_exists(i, h, -1):
                    dve.wait_ge(rstd_ready, c)
                    nc.vector.scalar_tensor_tensor(out=shift[h1][:, :], in0=mean_var[h1][:, :, 0], scalar=-1.0,
                                                   in1=rstd[h1][:, :], op0=ALU.mult, op1=ALU.mult
                                                   ).then_inc(shift_ready, 1)
                if chunk_exists(i, h, 1):
                    dve.wait_ge(rz_ready, c + 2)
                    if chunk_exists(i, h, -1):
                        dve.wait_ge(y_ready, c)
                    nc.vector.tensor_tensor(
                        attn[h1][:, :, :].rearrange("p t (h d) -> p t h d", d=HEAD_DIM),
                        node_ps[h1][:, :, 0:DIM].rearrange("p t (h d) -> p t h d", d=HEAD_DIM),
                        rz[h1][:, :, :].unsqueeze(3).to_broadcast([n, CHUNK, HEADS, HEAD_DIM]),
                        ALU.mult).then_inc(attn_ready, 1)
                if chunk_exists(i, h):
                    dve.wait_ge(y_ready, c + 1)
                    for t in range(CHUNK):
                        last = nc.vector.bn_stats(stats[h][:, t, :], y[:, bass.ds(CHUNK * c + t, 1), :]
                                                  .rearrange("p a d -> p (a d)"))
                    last.then_inc(stats_ready, 1)
                if chunk_exists(i, h):
                    dve.wait_ge(stats_ready, c + 1)
                    dve.sem_inc(aggregates_begun, 1)
                    for t in range(CHUNK):
                        last = nc.vector.bn_aggr(mean_var[h][:, t, :], stats[h][:, t, :])
                    last.then_inc(var_ready, 1)

            all_chunks(dve, node_step, -1, CHUNKS)

        @block.scalar
        def _(act):
            def stage(i, h, again):
                if again:
                    act.wait_ge(kv_written[h], 16 * i)
                for t in range(CHUNK):
                    act.wait_ge(table_ps_ready, CHUNK * (2 * i + h) + (t + 1))
                    nc.scalar.copy(kv_stage[:, h, t, :], table_ps[t][:, 0:2 * DIM])
                    nc.scalar.copy(q_rest[:, bass.ds(CHUNK * (2 * i + h) + t, 1), :].rearrange("p a d -> p (a d)"),
                                   table_ps[t][:, 2 * DIM:3 * DIM]).then_inc(table_staged, 1)

            def high_part(i):
                t = bass.ds(2 * CHUNK * i, 2 * CHUNK)
                act.wait_ge(table_staged, 2 * CHUNK * i + 2 * CHUNK)
                nc.scalar.copy(q_parts[:, t, 0, :], q_rest[:, t, :]).then_inc(q_high_ready, 1)

            def middle_part(i):
                t = bass.ds(2 * CHUNK * i, 2 * CHUNK)
                act.wait_ge(q_rest_ready, i + 1)
                nc.scalar.copy(q_parts[:, t, 1, :], q_rest[:, t, :]).then_inc(q_middle_ready, 1)

            def copy_indices(s, g):
                nc.scalar.copy(idx[s][:, :], src_sb[:, bass.ds(GROUP_TILES * g, GROUP_TILES)]
                               ).then_inc(idx_ready, 1)

            for h in range(2):
                stage(0, h, False)
            high_part(0)
            act.wait_ge(src_ready, 16)
            for s in range(SLOTS):
                copy_indices(s, s)
            with act.Fori(1, CHUNKS // 2) as i:
                for h in range(2):
                    stage(i, h, True)
                middle_part(i - 1)
                high_part(i)
            middle_part(CHUNKS // 2 - 1)

            passes = number_of_passes(act)
            with act.Fori(0, passes) as p:
                act.wait_ge(windows_ready, 2 * p + 1)

                def step(i, u):
                    b = u % 2
                    if exists(i, u, -1) and exists(i, u, 3):
                        act.wait_ge(kv_ready[slot(u, 3)], 64 * slot_uses(0, i, u, -1))
                        copy_indices(slot(u, 3), SLOTS * i + (u + 3))
                    if exists(i, u, 2):
                        act.wait_ge(hot_ps_ready, done(p, i, u, 2))
                        if exists(i, u):
                            act.wait_ge(q_ps_ready, done(p, i, u))
                        nc.scalar.copy(hot_t[b][:, :], hot_ps[b]).then_inc(hot_t_ready, 1)
                    if exists(i, u):
                        act.wait_ge(clipped_ready, done(p, i, u))
                        if exists(i, u, -2):
                            act.wait_ge(sum_ps_ready, done(p, i, u, -2))
                        nc.scalar.activation(msg[b][:, :, DIM:MSG], clipped[b][:, :, :], ACT.Exp,
                                             scale=SCALE).then_inc(exp_ready, 1)

                all_groups(act, step, -2, GROUPS - 1)
                for s in range(SLOTS):
                    act.wait_ge(msg_ready, p * GROUPS + GROUPS)
                    copy_indices(s, s)

            n = NODE_PARTITIONS

            def node_step(i, h):
                c = 2 * i + h
                h1 = 1 - h
                if chunk_exists(i, h, -1):
                    act.wait_ge(shift_ready, c)
                    for t in range(CHUNK):
                        row = y[:, bass.ds(CHUNK * (c - 1) + t, 1), :].rearrange("p a d -> p (a d)")
                        last = nc.scalar.activation(row, row, ACT.Identity,
                                                    bias=shift[h1][:, t:t + 1], scale=rstd[h1][:, t:t + 1])
                    last.then_inc(normed_ready, 1)
                if chunk_exists(i, h):
                    act.wait_ge(var_ready, c + 1)
                    nc.scalar.activation(std[h][:, :], mean_var[h][:, :, 1], ACT.Sqrt,
                                         bias=eps[0:n, 0:1]).then_inc(std_ready, 1)

            all_chunks(act, node_step, 0, CHUNKS)

        @block.tensor
        def _(pe):
            pe.wait_ge(weights_ready, 32)
            pe.wait_ge(ids_made, 2)

            def project(i, h, again):
                pe.wait_ge(x_ready[h], 16 * i + 16)
                for t in range(CHUNK):
                    if again or h:
                        pe.wait_ge(table_staged, CHUNK * (2 * i + h) + (t + 1 - CHUNK))
                    nc.tensor.matmul(table_ps[t], x_buf[h][:, t * P:(t + 1) * P], w_kvq,
                                     start=True, stop=True).then_inc(table_ps_ready, 1)

            for h in range(2):
                project(0, h, False)
            with pe.Fori(1, CHUNKS // 2) as i:
                for h in range(2):
                    project(i, h, True)

            passes = number_of_passes(pe)
            pe.wait_ge(constants_ready, 1)
            pe.wait_ge(identity_ready, 1)
            pe.wait_ge(table_staged, NODE_TILES)
            with pe.Fori(0, passes) as p:
                pe.wait_ge(windows_ready, 2 * p + 1)

                def step(i, u):
                    s1, b1 = slot(u, 1), (u + 1) % 2
                    if exists(i, u, 1):
                        pe.wait_ge(edge_ready[s1], 16 * slot_uses(p, i, u, 1))
                        if exists(i, u, -1):
                            pe.wait_ge(kqe_done, done(p, i, u, -1))
                        for j in range(GROUP_TILES):
                            last = nc.tensor.matmul(e_ps[b1][:, j * DIM:(j + 1) * DIM],
                                                    edge[s1][:, j * TILE:(j + 1) * TILE], w_edge,
                                                    start=True, stop=True)
                        last.then_inc(e_ps_ready, 1)
                    if exists(i, u, 2):
                        pe.wait_ge(hot_bf_ready, done(p, i, u, 2))
                        if exists(i, u):
                            pe.wait_ge(hot_t_ready, done(p, i, u))
                        nc.tensor.matmul(hot_ps[u % 2], hot_bf[u % 2][:, :, :].rearrange("p t n -> p (t n)"),
                                         identity_bf[:, :], start=True, stop=True).then_inc(hot_ps_ready, 1)
                    if exists(i, u, 1):
                        pe.wait_ge(hot_t_ready, done(p, i, u, 1))
                        pe.wait_ge(q_ready[s1], 64 * slot_uses(p, i, u, 1))
                        if exists(i, u, -1):
                            pe.wait_ge(kq_done, done(p, i, u, -1))
                        for k in range(Q_PARTS):
                            last = nc.tensor.matmul(q_ps[b1].rearrange("p (t d) -> p t d", d=DIM), hot_t[b1][:, :],
                                                    q_diag[s1][:, :, k, :], start=(k == 0), stop=(k == Q_PARTS - 1))
                        last.then_inc(q_ps_ready, 1)
                    if exists(i, u, -1):
                        pe.wait_ge(hot_ready, done(p, i, u, -1))
                        pe.wait_ge(msg_ready, done(p, i, u, -1))
                        if exists(i, u, -3):
                            pe.wait_ge(acc_done, done(p, i, u, -3))
                        for j in range(GROUP_TILES):
                            last = nc.tensor.matmul(sum_ps[b1], msg[b1][:, j, :], hot[slot(u, -1)][:, j, :],
                                                    start=(j == 0), stop=(j == GROUP_TILES - 1))
                        last.then_inc(sum_ps_ready, 1)

                all_groups(pe, step, -2, GROUPS)

            pe.wait_ge(acc_done, passes * GROUPS)
            acc_by_tile = acc[:, :].rearrange("m (p t) -> m t p", t=NODE_TILES)

            for c in range(CHUNKS):
                if c >= 2:
                    pe.wait_ge(attn_ready, c - 1)
                for t in range(CHUNK):
                    last = nc.tensor.transpose(node_ps[c % 2][:, t, 0:MSG],
                                               acc_by_tile[:, CHUNK * c + t, 0:NODE_PARTITIONS],
                                               identity[0:MSG, 0:MSG])
                last.then_inc(node_ps_ready, 1)


def kernel(x, src, dst, edge_attr_96, L0_gnn_Wq, L0_gnn_bq, L0_gnn_Wk, L0_gnn_bk, L0_gnn_We, L0_gnn_be,
           L0_gnn_Wv, L0_gnn_bv):
    import numpy as np
    import concourse.bacc as bacc
    from concourse.bass_utils import run_bass_kernel_spmd

    x, src, dst, edges = (np.asarray(a) for a in (x, src, dst, edge_attr_96))
    pad_edges = TILES * TILE - EDGES
    x_pad = np.concatenate([x, np.zeros((NODES_PAD - NODES, DIM), x.dtype)])
    x_tiles = x_pad.reshape(P, CHUNKS, CHUNK, DIM).transpose(1, 3, 2, 0).reshape(CHUNKS, DIM, CHUNK * P)
    edges_pad = np.concatenate([edges, np.zeros((pad_edges, DIM), edges.dtype)])
    edge_tiles = edges_pad.reshape(GROUPS, GROUP, DIM).transpose(0, 2, 1)
    src_pad = np.concatenate([src, np.zeros(pad_edges, src.dtype)])
    dst_pad = np.concatenate([dst, np.full(pad_edges, NODES, dst.dtype)])
    weights = np.concatenate([
        np.concatenate([np.asarray(w) for w in (L0_gnn_Wk, L0_gnn_Wv, L0_gnn_Wq, L0_gnn_We)], axis=1),
        np.concatenate([np.asarray(b) for b in (L0_gnn_bk, L0_gnn_bv, L0_gnn_bq, L0_gnn_be)])[None, :]])
    arrays = {
        "x_tiles": x_tiles,
        "x_rows": x.reshape(NODE_PARTITIONS, NODE_TILES, DIM),
        "edge_tiles": edge_tiles,
        "src": src_pad.reshape(TILES, TILE).T,
        "dst": dst_pad.reshape(TILES, TILE).T,
        "first_dst": dst_pad[::GROUP][None, :],
        "weights": weights,
    }
    arrays = {name: np.ascontiguousarray(a) for name, a in arrays.items()}
    nc = bacc.Bacc("TRN2", target_bir_lowering=False, num_devices=1)
    args = [nc.dram_tensor(f"in_{name}", a.shape, mybir.dt.from_np(a.dtype), kind="ExternalInput").ap()
            for name, a in arrays.items()]
    out = nc.dram_tensor("out_nodes", (NODE_PARTITIONS, NODE_TILES, DIM), mybir.dt.float32,
                         kind="ExternalOutput").ap()
    gnn_resnorm(nc, *args, out)
    r = run_bass_kernel_spmd(nc, [{f"in_{name}": a for name, a in arrays.items()}], core_ids=[0])
    return r.results[0]["out_nodes"].reshape(NODES, DIM)
```
